# Optimizing a Trainium2 kernel written in Bass

```python
import numpy as np
import jax
import jax.numpy as jnp

def _softmax(x, axis=-1):
    return jax.nn.softmax(x, axis=axis)

def _gelu(x):
    return jax.nn.gelu(x, approximate=True)

def _silu(x):
    return jax.nn.silu(x)

def _sigmoid(x):
    return jax.nn.sigmoid(x)

def _layernorm(x, axis=-1, eps=1e-05):
    m = jnp.mean(x, axis=axis, keepdims=True)
    v = jnp.var(x, axis=axis, keepdims=True)
    return (x - m) / jnp.sqrt(v + eps)

def _scatter_add(tgt, idx, src, axis=0):
    return tgt.at[idx].add(src)

def _segment_sum(src, seg, n):
    return jax.ops.segment_sum(src, seg, n)
kernel_name = 'mk_sandwich_d1_jaxref_r4_2e9ffb'

def setup_inputs(seed: int=0):
    np.random.seed(seed)
    _w = jnp.asarray

    def _L0_attn_setup():
        import math
        import jax, jax.numpy as jnp
        import numpy as np
        N_HEADS = 16
        D_EMBED = 256
        key = jax.random.key(seed)
        ks = jax.random.split(key, 5)
        b, l, d = (2, 512, D_EMBED)
        return {'x': jax.random.normal(ks[0], (b, l, d), dtype=jnp.float32), 'w_in': jax.random.normal(ks[1], (3 * d, d), dtype=jnp.float32) * 0.02, 'b_in': jax.random.normal(ks[2], (3 * d,), dtype=jnp.float32) * 0.02, 'w_out': jax.random.normal(ks[3], (d, d), dtype=jnp.float32) * 0.02, 'b_out': jax.random.normal(ks[4], (d,), dtype=jnp.float32) * 0.02}
    _L0_attn_in = _L0_attn_setup()

    def _L0_ffn_setup():
        import jax, jax.numpy as jnp
        import numpy as np
        B, S, D, F, E, R = (4, 512, 256, 1024, 8, 4)
        key = jax.random.key(seed)
        ks = jax.random.split(key, 8)
        s_in = 1.0 / np.sqrt(D)
        s_ff = 1.0 / np.sqrt(F)
        return {'hidden_states': jax.random.normal(ks[0], (B, S, D), jnp.float32), 'gate_W': jax.random.normal(ks[1], (E, D), jnp.float32) * s_in, 'gate_b': jnp.zeros((E,), jnp.float32), 'wi_W': jax.random.normal(ks[2], (F, D), jnp.float32) * s_in, 'wi_b': jnp.zeros((F,), jnp.float32), 'wo_W': jax.random.normal(ks[3], (D, F), jnp.float32) * s_ff, 'wo_b': jnp.zeros((D,), jnp.float32), 'lora_A': jax.random.normal(ks[4], (E, R, D), jnp.float32) * s_in, 'lora_B': jax.random.normal(ks[5], (E, F, R), jnp.float32) * 0.02}
    _L0_ffn_in = _L0_ffn_setup()
    _d = {'L0_attn_x': _L0_attn_in['x'], 'L0_attn_w_in': _L0_attn_in['w_in'], 'L0_attn_b_in': _L0_attn_in['b_in'], 'L0_attn_w_out': _L0_attn_in['w_out'], 'L0_attn_b_out': _L0_attn_in['b_out'], 'L0_ffn_gate_W': _L0_ffn_in['gate_W'], 'L0_ffn_gate_b': _L0_ffn_in['gate_b'], 'L0_ffn_wi_W': _L0_ffn_in['wi_W'], 'L0_ffn_wi_b': _L0_ffn_in['wi_b'], 'L0_ffn_wo_W': _L0_ffn_in['wo_W'], 'L0_ffn_wo_b': _L0_ffn_in['wo_b'], 'L0_ffn_lora_A': _L0_ffn_in['lora_A'], 'L0_ffn_lora_B': _L0_ffn_in['lora_B']}
    _x0 = _d['L0_attn_x']
    _d['L0_attn_x'] = jax.random.normal(jax.random.fold_in(jax.random.key(seed), 1), (8, 512, 256), dtype=_x0.dtype)
    del _x0
    return _d

def reference(L0_attn_x, L0_attn_w_in, L0_attn_b_in, L0_attn_w_out, L0_attn_b_out, L0_ffn_gate_W, L0_ffn_gate_b, L0_ffn_wi_W, L0_ffn_wi_b, L0_ffn_wo_W, L0_ffn_wo_b, L0_ffn_lora_A, L0_ffn_lora_B):

    def _L0_attn_ref(x, w_in, b_in, w_out, b_out):
        import math
        import jax, jax.numpy as jnp
        import numpy as np
        N_HEADS = 16
        D_EMBED = 256
        b, l, d = x.shape
        h = N_HEADS
        scale = 1.0 / math.sqrt(d // h)
        x_proj = (x @ w_in.T + b_in).reshape(b, l, h, -1)
        q, k, v = jnp.split(x_proj, 3, axis=-1)
        att = jnp.einsum('blhd,bmhd->blmh', q, k) * scale
        att = jax.nn.softmax(att, axis=2)
        opt = jnp.einsum('blmh,blhd->blhd', att, v).reshape(b, l, d)
        return opt @ w_out.T + b_out

    def _L0_ffn_ref(hidden_states, gate_W, gate_b, wi_W, wi_b, wo_W, wo_b, lora_A, lora_B):
        import jax, jax.numpy as jnp
        import numpy as np
        B, S, D, F, E, R = (4, 512, 256, 1024, 8, 4)
        x = hidden_states
        logits = jnp.einsum('bsd,ed->bse', x, gate_W) + gate_b
        top1 = jnp.argmax(jax.nn.softmax(logits, axis=-1), axis=-1)
        base = jnp.einsum('bsd,fd->bsf', x, wi_W) + wi_b
        out = jnp.zeros_like(x)
        for i in range(lora_A.shape[0]):
            lora = jnp.einsum('bsr,fr->bsf', jnp.einsum('bsd,rd->bsr', x, lora_A[i]), lora_B[i])
            inter = jax.nn.relu(base + lora)
            expert_out = jnp.einsum('bsf,df->bsd', inter, wo_W) + wo_b
            mask = (top1 == i).astype(x.dtype)[..., None]
            out = out + mask * expert_out
        return out
    x = L0_attn_x
    x = x + _layernorm(_L0_attn_ref(_layernorm(x, axis=-1), L0_attn_w_in, L0_attn_b_in, L0_attn_w_out, L0_attn_b_out), axis=-1)
    x = x + _layernorm(_L0_ffn_ref(_layernorm(x, axis=-1), L0_ffn_gate_W, L0_ffn_gate_b, L0_ffn_wi_W, L0_ffn_wi_b, L0_ffn_wo_W, L0_ffn_wo_b, L0_ffn_lora_A, L0_ffn_lora_B), axis=-1)
    return x

_drawn_inputs = setup_inputs


def setup_inputs(seed=0):
    import zlib

    import numpy as np

    out = dict(_drawn_inputs(seed))
    spreads = {'L0_ffn_gate_b': (0.0, 0.1), 'L0_ffn_wi_b': (0.0, 0.1), 'L0_ffn_wo_b': (0.0, 0.1)}
    factors = {}
    for name, (base, spread) in spreads.items():
        noise = np.random.default_rng([zlib.crc32(name.encode()), seed]).standard_normal(out[name].shape)
        drawn = base * np.exp(spread * noise) if base else spread * noise
        out[name] = jnp.asarray(drawn.astype(out[name].dtype))
    for name, factor in factors.items():
        out[name] = (out[name] * factor).astype(out[name].dtype)
    return out
```

```python
from contextlib import ExitStack

import numpy as np
import concourse.bass as bass
from concourse import mybir

F32 = mybir.dt.float32
F32R = mybir.dt.float32r
ALU = mybir.AluOpType
ACT = mybir.ActivationFunctionType
AX_X = mybir.AxisListType.X

B, L, D, H, F, E, R = 8, 512, 256, 16, 1024, 8, 4
NT = L // 128
EPS = 1e-5
PIECES = 5
XB = 4
GROUPS = 32


class Sem:

    def __init__(self, sem):
        self.sem, self.n = sem, 0


class Queue:

    def __init__(self):
        self.items, self.seen = [], {}

    def do(self, fn, sem=None, by=1):
        if sem is None:
            self.items.append(fn)
            return None
        sem.n += by
        self.items.append(lambda e: fn(e).then_inc(sem.sem, by))
        return (sem, sem.n)

    def wait(self, *points):
        for p in points:
            if p is None:
                continue
            sem, n = p
            if self.seen.get(sem, 0) >= n:
                continue
            self.seen[sem] = n
            self.items.append(lambda e, s=sem.sem, v=n: e.wait_ge(s, v))

    def play(self, e):
        for fn in self.items:
            fn(e)


def sandwich(nc, x, wqk, wv, bqk, wout, wgate, wi, lora, wib, wo, brows, ident, out):
    with ExitStack() as ctx:
        def sb(name, shape, dt=F32):
            return ctx.enter_context(nc.sbuf_tensor(name, shape, dt))

        def sem(name):
            return Sem(ctx.enter_context(nc.semaphore(name)))

        ps = [ctx.enter_context(nc.psum_tensor(f"ps{i}", [128, 2, 512], F32)) for i in range(3)]
        pu = [ctx.enter_context(nc.psum_tensor(f"pu{i}", [128, 512], F32)) for i in range(2)]

        xb = sb("xb", [128, XB, NT, D])
        xn = sb("xn", [128, NT, D])
        xnT = sb("xnT", [128, 2, 2, L], F32R)
        qk = sb("qk", [128, 4, 2, L], F32R)
        stack = sb("stack", [128, PIECES, 2, 2, L], F32R)
        vo = sb("vo", [128, 2, NT, D])
        oT = sb("oT", [128, 2, L])
        y = sb("y", [128, NT, D])
        y2 = sb("y2", [128, NT, D])
        yT = sb("yT", [128, 2, 2, L], F32R)
        inter = sb("inter", [128, 2, 8, L], F32R)
        wqk_r = sb("wqk_r", [128, 2, 2, 512], F32R)
        wv_r = sb("wv_r", [128, 2, 2, 256], F32R)
        wg_r = sb("wg_r", [128, 2, 2, 40], F32R)
        wi_r = sb("wi_r", [128, 2, 2, F], F32R)
        wo_r = sb("wo_r", [128, 2, 8, D], F32R)
        lb_r = sb("lb_r", [98, F], F32R)
        br_r = sb("br_r", [2, 808], F32R)
        wout_s = sb("wout_s", [128, 2, D])
        bqk_s = sb("bqk_s", [128, 4])
        wg_s = sb("wg_s", [128, 2, 40])
        id_s = sb("id_s", [128, 128])
        ones_r = sb("ones_r", [2, 128], F32R)
        ones = sb("ones", [2, 128])
        halves = sb("halves", [128, NT])
        w8 = sb("w8", [128, NT, E])
        nmax = sb("nmax", [128, 4, 2])
        ssum = sb("ssum", [128, 2, NT, H])
        srec = sb("srec", [128, NT, H])
        sone = sb("sone", [128, NT, H])
        st6 = [sb(f"st6_{i}", [128, NT, 6]) for i in range(3)]
        mv = [sb(f"mv_{i}", [128, NT, 2]) for i in range(3)]
        nmr = [sb(f"nmr_{i}", [128, 3, NT]) for i in range(3)]
        gs = sb("gs", [128, NT, 40])
        g8 = sb("g8", [128, 6, NT, E])
        g1 = sb("g1", [128, 5, NT])
        ml = sb("ml", [128, NT, E, R])
        mh = sb("mh", [128, NT, 32], F32R)
        ms = sb("ms", [128, NT, 98])
        lt_r = sb("lt_r", [98, L], F32R)

        s_w = [sem(f"s_w{i}") for i in range(12)]
        s_x = [sem(f"s_x{i}") for i in range(XB)]
        s_st = [sem(f"s_st{i}") for i in range(PIECES)]
        s_out = [sem(f"s_out{i}") for i in range(XB)]
        s_row = sem("s_row")
        s_const = sem("s_const")
        s_split_v = sem("s_split_v")
        s_split_p = sem("s_split_p")
        s_score = sem("s_score")
        s_max = sem("s_max")
        s_exp = sem("s_exp")
        s_unit = sem("s_unit")
        s_high = sem("s_high")
        s_low = sem("s_low")
        s_stat = sem("s_stat")
        s_norm = sem("s_norm")
        s_ratio = sem("s_ratio")
        s_gate = sem("s_gate")
        s_gexp = sem("s_gexp")

        PE, AC, DV, PO, SP = (Queue() for _ in range(5))

        def load(i, dst, src):
            return SP.do(lambda e: e.dma_start(dst, src), s_w[i], 16)

        free_x = [None] * XB
        x_here = {}

        def load_x(b):
            SP.wait(free_x[b % XB])
            x_here[b] = SP.do(lambda e: e.dma_start(
                xb[:, b % XB], x[b].rearrange("(t p) d -> p t d", p=128)), s_x[b % XB], 16)

        load_x(0)
        wqk_st = oT[:].rearrange("p a b -> p (a b)").rearrange("p (c m) -> p c m", c=2)
        wv_st = y[:, 0:2, :]
        c_wqk = load(0, wqk_st, wqk)
        c_id = load(1, id_s[:], ident)
        c_bqk = load(2, bqk_s[:], bqk)
        c_wv = load(3, wv_st, wv)
        rows_st = xn[0:1, 0:4, :].rearrange("p a b -> p (a b)")[:, 0:808]
        c_rows = load(4, rows_st, brows)
        load_x(1)
        wi_st = vo[:, 1, :, :].rearrange("p a b -> p (a b)")
        wo_st = xb[:, 2:4].rearrange("p x t d -> p (x t d)").rearrange("p (f d) -> p f d", f=8)
        c_wo = load(5, wo_st, wo)
        c_wi0 = load(6, wi_st, wi[:, 0, :])
        c_wg = load(8, wg_s[:], wgate)
        c_wout = load(9, wout_s[:], wout)

        PO.do(lambda e: e.memset(ones[:], 1.0), s_const)
        PO.do(lambda e: e.memset(halves[:], -0.5), s_const)
        for i in range(E):
            PO.do(lambda e, i=i: e.memset(w8[:, :, i:i + 1], float(E - i)), s_const)
        c_const = PO.do(lambda e: e.memset(ms[:, :, 96:98], 1.0), s_const)
        DV.wait(c_const)
        c_ones = DV.do(lambda e: e.tensor_copy(ones_r[:], ones[:]), s_split_v)

        DV.wait(c_wqk)
        for (lo, hi, k) in ((0, 256, 0.25), (256, 512, 1.0)):
            a = DV.do(lambda e, lo=lo, hi=hi, k=k: e.tensor_scalar(
                wqk_r[:, 0, :, lo:hi], wqk_st[:, :, lo:hi], k, None, ALU.mult), s_split_v)
            DV.wait(a)
            c_sqk = DV.do(lambda e, lo=lo, hi=hi, k=k: e.scalar_tensor_tensor(
                wqk_r[:, 1, :, lo:hi], wqk_st[:, :, lo:hi], k, wqk_r[:, 0, :, lo:hi].bitcast(F32),
                ALU.mult, ALU.subtract), s_split_v)
        DV.wait(c_bqk)
        c_bq = DV.do(lambda e: e.tensor_scalar(bqk_s[:, 0:2], bqk_s[:, 0:2], 0.25, None, ALU.mult), s_split_v)

        def split(q, sem_, high, low, whole):
            a = q.do(lambda e: e.tensor_copy(high, whole), sem_)
            q.wait(a)
            return q.do(lambda e: e.tensor_tensor(low, whole, high.bitcast(F32), ALU.subtract), sem_)

        DV.wait(c_wv)
        c_sv = split(DV, s_split_v, wv_r[:, 0], wv_r[:, 1], wv_st)
        DV.wait(c_rows)
        a = DV.do(lambda e: e.tensor_copy(br_r[0:1, :], rows_st), s_split_v)
        DV.wait(a)
        rl = inter[0:1, 0, 0:2, :].rearrange("p a b -> p (a b)")
        a = DV.do(lambda e: e.tensor_tensor(rl[:, 0:808], rows_st, br_r[0:1, :].bitcast(F32), ALU.subtract), s_split_v)
        SP.wait(a)
        c_brow = SP.do(lambda e: e.dma_start(br_r[1:2, :].bitcast(F32), rl[:, 0:808].bitcast(F32)), s_row, 16)
        BV, BO, BW, BG = (slice(0, 256), slice(256, 512), slice(512, 768), slice(768, 808))

        late = {}

        def split_late():
            PO.wait(c_wo)
            p = split(PO, s_split_p, wo_r[:, 0], wo_r[:, 1], wo_st)
            free_x[2] = free_x[3] = p
            late["wo"] = p
            PO.wait(c_wi0)
            p0 = split(PO, s_split_p, wi_r[:, 0, 0], wi_r[:, 1, 0], wi_st)
            yield
            SP.wait(p0)
            c = load(7, wi_st, wi[:, 1, :])
            PO.wait(c)
            p = split(PO, s_split_p, wi_r[:, 0, 1], wi_r[:, 1, 1], wi_st)
            SP.wait(p)
            free_v[1].append(p)
            late["wi"] = p
            PO.wait(c_wg)
            late["wg"] = split(PO, s_split_p, wg_r[:, 0], wg_r[:, 1], wg_s[:])
            lst = y[0:98].rearrange("p a b -> p (a b)")
            SP.wait(c_sv)
            c = load(10, lst[0:96], lora)
            c = load(10, lst[96:98], wib)
            PO.wait(c)
            a = PO.do(lambda e: e.tensor_copy(lb_r[:, :], lst), s_split_p)
            PO.wait(a)
            a = PO.do(lambda e: e.tensor_tensor(rl[:, :], lst[96:97], lb_r[96:97].bitcast(F32), ALU.subtract), s_split_p)
            PO.wait(a)
            a = PO.do(lambda e: e.tensor_tensor(lb_r[32:64], lst[32:64], lb_r[32:64].bitcast(F32), ALU.subtract),
                      s_split_p)
            PO.wait(a)
            SP.wait(a, c_brow)
            late["lb"] = SP.do(lambda e: e.dma_start(lb_r[97:98].bitcast(F32), rl[:, :].bitcast(F32)), s_row, 16)
            late["y"] = a
            yield

        unit_n = [0]
        unit_free = [[], []]
        evacs = []

        def unit(pe, evac):
            i = unit_n[0] % 2
            unit_n[0] += 1
            PE.wait(*unit_free[i])
            done = pe(pu[i])

            def later():
                unit_free[i] = evac(pu[i], done)
            evacs.append(later)

        def mm(out_, lhsT, rhs, start, stop, sem_=None):
            return PE.do(lambda e: e.matmul(out_, lhsT, rhs, start=start, stop=stop), sem_)

        def three(out_, lT, r, chunks, first=True, last=False, sem_=None):
            n = len(chunks)
            for i, c in enumerate(chunks):
                for j, (a, b_) in enumerate(((0, 0), (0, 1), (1, 0))):
                    end = last and i == n - 1 and j == 2
                    p = mm(out_, lT(a, c), r(b_, c), first and i == 0 and j == 0, end, sem_ if end else None)
            return p

        def transposes(src, c, ready):
            def pe(bank):
                PE.wait(c_id, *ready)
                for t in range(NT):
                    p = PE.do(lambda e, t=t: e.transpose(bank[:, t * 128:(t + 1) * 128],
                                                         src[:, t, c * 128:(c + 1) * 128], id_s[:]),
                              s_unit if t == NT - 1 else None)
                return p
            return pe

        def high_low(high, low, wait_free, got, bias=None, relu=False):
            def evac(bank, done):
                AC.wait(done, *wait_free)
                if relu:
                    h = AC.do(lambda e: e.activation(high, bank[:], ACT.Relu), s_high)
                elif bias is not None:
                    AC.wait(c_bq)
                    h = AC.do(lambda e: e.activation(high, bank[:], ACT.Identity, bias=bias), s_high)
                else:
                    h = AC.do(lambda e: e.activation(high, bank[:], ACT.Copy), s_high)
                DV.wait(h)
                hf = high.bitcast(F32)
                if relu:
                    p = DV.do(lambda e: e.scalar_tensor_tensor(low, bank[:], 0.0, hf, ALU.max, ALU.subtract), s_low)
                elif bias is not None:
                    p = DV.do(lambda e: e.scalar_tensor_tensor(low, bank[:], bias, hf, ALU.add, ALU.subtract), s_low)
                else:
                    p = DV.do(lambda e: e.tensor_tensor(low, bank[:], hf, ALU.subtract), s_low)
                got.append(p)
                return [p]
            return evac

        def stats(i, src, t, ready):
            DV.wait(*ready)
            a = DV.do(lambda e: e.bn_stats(st6[i][:, t, :], src[:, t, :]), s_stat)
            DV.wait(a)
            return DV.do(lambda e: e.bn_aggr(mv[i][:, t, :], st6[i][:, t, :]), s_stat)

        def rstd(i, ready):
            PO.wait(ready, c_const)
            PO.do(lambda e: e.tensor_scalar(nmr[i][:, 0, :], mv[i][:, :, 0], -1.0, None, ALU.mult), s_norm)
            a = PO.do(lambda e: e.tensor_scalar(nmr[i][:, 1, :], mv[i][:, :, 1], EPS, None, ALU.add), s_norm)
            PO.wait(a)
            a = PO.do(lambda e: e.tensor_tensor(nmr[i][:, 2, :], nmr[i][:, 1, :], halves[:], ALU.pow), s_norm)
            PO.wait(a)
            return a

        def norm(i, dst, src, t):
            return PO.do(lambda e: e.tensor_scalar(dst[:, t, :], src[:, t, :], nmr[i][:, 0, t:t + 1],
                                                   nmr[i][:, 2, t:t + 1], ALU.add, ALU.mult), s_norm)

        free_v = [[], []]
        v_here = {}
        piece_here = {}
        piece_free = [None] * PIECES
        xnT_free, xn_free, qk_free = [], [], []
        pre_done = set()

        def pre(b):
            xs = xb[:, b % XB]
            while b not in x_here:
                yield "go"
            for t in range(NT):
                a = stats(0, xs, t, [x_here[b]] + last_rstd[0])
                if t % 2:
                    yield "go"
            last_rstd[0] = [rstd(0, a)]
            PO.wait(*xn_free)
            n = [norm(0, xn, xs, t) for t in range(NT)][-1]
            yield "go"
            if b:
                yield "go"
            hl = []
            free = list(xnT_free)
            for c in range(2):
                yield "unit"
                unit(transposes(xn, c, [n]), high_low(xnT[:, 0, c], xnT[:, 1, c], free, hl))
            yield "go"
            xn_free[:] = [unit_done(0)]
            got = []
            fr = list(qk_free)
            for m in range(4):
                yield "unit"
                part, c = m // 2, m % 2

                def pe(bank, m=m):
                    PE.wait(*hl, c_sqk)
                    return three(bank[:], lambda a, k: wqk_r[:, a, k, m * 128:(m + 1) * 128],
                                 lambda a, k: xnT[:, a, k, :], (0, 1), last=True, sem_=s_unit)
                unit(pe, high_low(qk[:, 2 * part, c], qk[:, 2 * part + 1, c], fr, got, bias=bqk_s[:, m:m + 1]))
            yield "go"
            last = []
            for j in range(4):
                ring = (4 * b + j) % PIECES
                SP.wait(got[-1], piece_free[ring])
                for p in range(2):
                    s = 2 * j + p
                    for t in range(4):
                        qa, ka = t // 2, 2 + t % 2
                        dst = stack[64 * p + t:64 * p + 64:4, ring].rearrange("p q c l -> p q (c l)")
                        src = qk[s:128:8, qa:ka + 1:ka - qa].rearrange("p q c l -> p q (c l)")
                        z = SP.do(lambda e, dst=dst, src=src: e.dma_start(dst.bitcast(F32), src.bitcast(F32)),
                                  s_st[ring], 16)
                piece_here[4 * b + j] = z
                last.append(z)
                if j < 3 and b:
                    need = 4 * b + j + 1 - PIECES
                    while need >= 0 and need not in piece_used:
                        yield "go"
            qk_free[:] = last
            for u in range(2):
                yield "unit"

                def pe(bank, u=u):
                    PE.wait(c_sv, c_brow, c_ones)
                    for k in range(2):
                        t = 2 * u + k
                        o = bank[:, k * 256:(k + 1) * 256]
                        three(o, lambda a, c: xnT[:, a, c, t * 128:(t + 1) * 128], lambda a, c: wv_r[:, a, c, :],
                              (0, 1))
                        p = mm(o, ones_r[:], br_r[:, BV], False, True, s_unit)
                    return p

                def evac(bank, done, u=u):
                    AC.wait(done, *free_v[b % 2])
                    p = AC.do(lambda e: e.activation(vo[:, b % 2, 2 * u:2 * u + 2, :].rearrange("p a b -> p (a b)"),
                                                     bank[:], ACT.Copy), s_high)
                    v_here[b] = p
                    return [p]
                unit(pe, evac)
            xnT_free[:] = [unit_done(0)]
            yield "go"
            pre_done.add(b)

        def unit_done(_):
            return (s_unit, s_unit.n)

        last_rstd = [[], [], []]
        piece_used = {}
        exp_done = {}
        oT_free, y_free, yT_free, inter_free, lt_free = [], [], [], [], []

        def ln_into(i, y, xs, done):
            for t in range(NT):
                a = stats(i, y, t, [done] + last_rstd[i])
                if t % 2:
                    yield "go"
            rstd(i, a)
            for t in range(NT):
                n = norm(i, y, y, t)
            PO.wait(n)
            for t in range(NT):
                last = PO.do(lambda e, t=t: e.tensor_tensor(xs[:, t, :], xs[:, t, :], y[:, t, :], ALU.add), s_norm)
            last_rstd[i] = [last]
            yield "go"
            yield "go"

        def post(b):
            xs = xb[:, b % XB]
            v = vo[:, b % 2]
            DV.wait(exp_done[b], *last_ratio)
            a = DV.do(lambda e: e.reciprocal(srec[:], ssum[:, b % 2]), s_ratio)
            DV.wait(a)
            a = DV.do(lambda e: e.tensor_tensor(sone[:], ssum[:, b % 2], srec[:], ALU.mult), s_ratio)
            ssum_free[b % 2] = a
            PO.wait(a, v_here[b])
            for t in range(NT):
                vt = v[:, t, :].rearrange("p (h d) -> p h d", h=H)
                o = PO.do(lambda e, vt=vt, t=t: e.tensor_tensor(
                    vt, vt, sone[:, t, :].unsqueeze(2).to_broadcast([128, H, 16]), ALU.mult), s_norm)
            last_ratio[:] = [o]
            yield "go"
            yield "go"
            got = []
            fr = list(oT_free)
            for c in range(2):
                yield "unit"

                def evac(bank, done, c=c):
                    AC.wait(done, *fr)
                    p = AC.do(lambda e: e.activation(oT[:, c, :], bank[:], ACT.Copy), s_high)
                    got.append(p)
                    return [p]
                unit(transposes(v, c, [o]), evac)
            free_v[b % 2] = [unit_done(0)]
            yield "go"
            ys = []
            fr2 = list(y_free)
            for u in range(2):
                yield "unit"

                def pe(bank, u=u):
                    PE.wait(*got, c_wout, c_brow, c_ones)
                    for k in range(2):
                        t = 2 * u + k
                        o_ = bank[:, k * 256:(k + 1) * 256]
                        for c in range(2):
                            mm(o_, oT[:, c, t * 128:(t + 1) * 128], wout_s[:, c, :], c == 0, False)
                        p = mm(o_, ones_r[:], br_r[:, BO], False, True, s_unit)
                    return p

                def evac(bank, done, u=u):
                    AC.wait(done, late["y"], *fr2)
                    p = AC.do(lambda e: e.activation(y[:, 2 * u:2 * u + 2, :].rearrange("p a b -> p (a b)"),
                                                     bank[:], ACT.Copy), s_high)
                    ys.append(p)
                    return [p]
                unit(pe, evac)
            oT_free[:] = [unit_done(0)]
            yield "go"
            yield from ln_into(1, y, xs, ys[-1])
            for t in range(NT):
                a = stats(1, xs, t, last_rstd[1])
                if t % 2:
                    yield "go"
            rstd(1, a)
            n = [norm(1, y, xs, t) for t in range(NT)][-1]
            last_rstd[1] = [n]
            yield "go"
            yield "go"
            while b and b - 1 not in wi_done:
                yield "go"
            hl = []
            fr = list(yT_free)
            for c in range(2):
                yield "unit"
                unit(transposes(y, c, [n]), high_low(yT[:, 0, c], yT[:, 1, c], fr, hl))
            y_free[:] = [unit_done(0)]
            yield "go"
            gd = []
            yield "unit"

            def pe(bank):
                PE.wait(*hl, late["wg"])
                for t in range(NT):
                    o_ = bank[:, t * 40:(t + 1) * 40]
                    three(o_, lambda a_, c: yT[:, a_, c, t * 128:(t + 1) * 128], lambda a_, c: wg_r[:, a_, c, :],
                          (0, 1))
                    p = mm(o_, ones_r[:], br_r[:, BG], False, True, s_unit)
                return p

            def evac(bank, done):
                DV.wait(done, *gate_free)
                p = DV.do(lambda e: e.tensor_copy(gs[:].rearrange("p t g -> p (t g)"), bank[:, 0:160]), s_gate)
                gd.append(p)
                return [p]
            unit(pe, evac)
            yield "go"
            def dv(fn):
                p = DV.do(fn, s_gate)
                DV.wait(p)
                return p

            def wide(i):
                return g1[:, i, :].unsqueeze(2).to_broadcast([128, NT, E])
            lg = gs[:, :, 0:8]
            DV.wait(gd[0])
            dv(lambda e: e.tensor_reduce(g1[:, 0, :], lg, AX_X, ALU.max))
            a = dv(lambda e: e.tensor_tensor(g8[:, 0], lg, wide(0), ALU.subtract))
            AC.wait(a)
            ge = AC.do(lambda e: e.activation(g8[:, 1], g8[:, 0], ACT.Exp), s_gexp)
            yield "go"
            DV.wait(ge)
            dv(lambda e: e.tensor_reduce(g1[:, 1, :], g8[:, 1], AX_X, ALU.add))
            dv(lambda e: e.reciprocal(g1[:, 2, :], g1[:, 1, :]))
            dv(lambda e: e.tensor_tensor(g8[:, 2], g8[:, 1], wide(2), ALU.mult))
            dv(lambda e: e.tensor_reduce(g1[:, 3, :], g8[:, 2], AX_X, ALU.max))
            dv(lambda e: e.tensor_tensor(g8[:, 3], g8[:, 2], wide(3), ALU.is_equal))
            dv(lambda e: e.tensor_tensor(g8[:, 4], g8[:, 3], w8[:], ALU.mult))
            dv(lambda e: e.tensor_reduce(g1[:, 4, :], g8[:, 4], AX_X, ALU.max))
            dv(lambda e: e.tensor_tensor(g8[:, 5], g8[:, 4], wide(4), ALU.is_equal))
            DV.wait(*ml_free)
            dv(lambda e: e.tensor_tensor(ml[:], gs[:, :, 8:40].rearrange("p t (e r) -> p t e r", e=E),
                                         g8[:, 5].unsqueeze(3).to_broadcast([128, NT, E, R]), ALU.mult))
            mlf = ml[:].rearrange("p t e r -> p t (e r)")
            dv(lambda e: e.tensor_copy(mh[:], mlf))
            for k in range(2):
                dv(lambda e, k=k: e.tensor_copy(ms[:, :, 32 * k:32 * k + 32], mh[:].bitcast(F32)))
            a = dv(lambda e: e.tensor_tensor(ms[:, :, 64:96], mlf, mh[:].bitcast(F32), ALU.subtract))
            gate_free[:] = [a]
            yield "go"
            yield "unit"
            lt = []

            def pe(bank):
                PE.wait(a)
                for t in range(NT):
                    p = PE.do(lambda e, t=t: e.transpose(bank[0:98, t * 128:(t + 1) * 128], ms[:, t, :], id_s[:]),
                              s_unit if t == NT - 1 else None)
                ml_free[:] = [p]
                return p

            def evac(bank, done):
                AC.wait(done, *lt_free)
                p = AC.do(lambda e: e.activation(lt_r[:], bank[0:98, :], ACT.Copy), s_high)
                lt.append(p)
                return [p]
            unit(pe, evac)
            yield "go"
            operands[b] = (lt, xs)
            post_done.add(b)

        def feed(b):
            lt, xs = operands[b]
            got = []
            fr = list(inter_free)
            for f in range(8):
                yield "unit"

                def pe(bank, f=f):
                    PE.wait(*lt, late["wi"], late["lb"])
                    three(bank[:], lambda a_, c: wi_r[:, a_, c, f * 128:(f + 1) * 128],
                          lambda a_, c: yT[:, a_, c, :], (0, 1))
                    return mm(bank[:], lb_r[:, f * 128:(f + 1) * 128], lt_r[:], False, True, s_unit)
                unit(pe, high_low(inter[:, 0, f, :], inter[:, 1, f, :], fr, got, relu=True))
            yT_free[:] = lt_free[:] = [unit_done(0)]
            wi_done.add(b)
            yield "go"
            ys = []
            for u in range(2):
                yield "unit"

                def pe(bank, u=u):
                    PE.wait(got[-1], late["wo"])
                    for k in range(2):
                        t = 2 * u + k
                        o_ = bank[:, k * 256:(k + 1) * 256]
                        three(o_, lambda a_, f: inter[:, a_, f, t * 128:(t + 1) * 128],
                              lambda a_, f: wo_r[:, a_, f, :], range(8))
                        p = mm(o_, ones_r[:], br_r[:, BW], False, True, s_unit)
                    return p

                def evac(bank, done, u=u):
                    AC.wait(done, *last_rstd[2])
                    p = AC.do(lambda e: e.activation(y2[:, 2 * u:2 * u + 2, :].rearrange("p a b -> p (a b)"),
                                                     bank[:], ACT.Copy), s_high)
                    ys.append(p)
                    return [p]
                unit(pe, evac)
                if u == 0:
                    yield "go"
            inter_free[:] = [unit_done(0)]
            yield "go"
            yield from ln_into(2, y2, xs, ys[-1])
            SP.wait(last_rstd[2][0])
            free_x[b % XB] = SP.do(lambda e: e.dma_start(out[b].rearrange("(t p) d -> p t d", p=128), xs),
                                   s_out[b % XB], 16)
            stores.append(free_x[b % XB])
            feed_done.add(b)

        operands, post_done, wi_done, feed_done = {}, set(), set(), set()
        last_ratio, gate_free, ml_free, stores = [], [], [], []
        ssum_free = [None, None]

        score_done, max_done, group_exp = {}, {}, {}

        def where(g):
            b, k = divmod(g, GROUPS)
            return b, k // 8, k % 8 // 2, k % 2

        def scores(g):
            b, j, t, c = where(g)
            piece = 4 * b + j
            PE.wait(piece_here[piece])
            if g >= 3:
                PE.wait(group_exp[g - 3])
            bank = ps[g % 3]
            ring = piece % PIECES
            for p in range(2):
                q = slice(64 * p, 64 * p + 64)
                z = PE.do(lambda e, p=p, q=q: e.matmul(bank[:, p, :], stack[q, ring, 0, c, t * 128:(t + 1) * 128],
                                                       stack[q, ring, 1, c, :], start=True, stop=True),
                          s_score if p else None)
            score_done[g] = z
            if k_last(g):
                piece_used[piece] = z
                piece_free[ring] = z

        def k_last(g):
            return g % 8 == 7

        def maxima(g):
            DV.wait(score_done[g])
            if g >= 4:
                DV.wait(group_exp[g - 4])
            max_done[g] = DV.do(lambda e: e.tensor_reduce(nmax[:, g % 4, :], ps[g % 3][:], AX_X, ALU.max,
                                                          negate=True), s_max)

        def exps(g):
            b, j, t, c = where(g)
            AC.wait(max_done[g], ssum_free[b % 2] if g % GROUPS == 0 else None)
            for p in range(2):
                h = 8 * c + 2 * j + p
                z = AC.do(lambda e, p=p, h=h: e.activation(ps[g % 3][:, p, :], ps[g % 3][:, p, :], ACT.Exp,
                                                           bias=nmax[:, g % 4, p:p + 1],
                                                           accum_out=ssum[:, b % 2, t, h:h + 1]), s_exp)
            group_exp[g] = z
            exp_done[b] = z

        threads = []

        def slot(g):
            attn = g is not None
            total = B * GROUPS
            if attn and g + 2 < total:
                scores(g + 2)
            if attn and g + 1 < total:
                maxima(g + 1)
            now, evacs[:] = evacs[:], []
            for fn in now:
                fn()
            if attn:
                exps(g)
            granted = False
            for th in list(threads):
                if not th["ready"]():
                    continue
                if th["want"] == "unit":
                    if granted:
                        continue
                    granted = True
                try:
                    th["want"] = next(th["gen"])
                except StopIteration:
                    threads.remove(th)

        def start(gen, ready=lambda: True):
            threads.append({"gen": gen, "want": "go", "ready": ready})

        def start_post(b):
            start(post(b), lambda: b == 0 or b - 1 in post_done)
            start(feed(b), lambda: b in post_done and (b == 0 or b - 1 in feed_done))

        def late_thread():
            for _ in split_late():
                yield "go"

        start(pre(0))
        while 0 not in pre_done:
            slot(None)
        load_x_next = 2
        scores(0)
        scores(1)
        maxima(0)
        start(late_thread())
        for g in range(B * GROUPS):
            b, k = divmod(g, GROUPS)
            if k == 0:
                if b:
                    start_post(b - 1)
                if b + 1 < B:
                    start(pre(b + 1))
            if load_x_next < B and "wo" in late and (load_x_next < XB or load_x_next - XB in feed_done):
                load_x(load_x_next)
                load_x_next += 1
            if k == GROUPS - 3 and b + 1 < B:
                while b + 1 not in pre_done:
                    slot(None)
            slot(g)
        start_post(B - 1)
        while threads or evacs:
            slot(None)
        SP.wait(*stores)

        block = ctx.enter_context(nc.Block())

        @block.sync
        def _(e):
            SP.play(e)

        @block.tensor
        def _(e):
            PE.play(e)

        @block.scalar
        def _(e):
            AC.play(e)

        @block.vector
        def _(e):
            DV.play(e)

        @block.gpsimd
        def _(e):
            PO.play(e)


def kernel(L0_attn_x, L0_attn_w_in, L0_attn_b_in, L0_attn_w_out, L0_attn_b_out, L0_ffn_gate_W, L0_ffn_gate_b,
           L0_ffn_wi_W, L0_ffn_wi_b, L0_ffn_wo_W, L0_ffn_wo_b, L0_ffn_lora_A, L0_ffn_lora_B):
    import concourse.bacc as bacc
    from concourse.bass_utils import run_bass_kernel_spmd

    def arr(a):
        return np.asarray(a)

    def chunks(wT):
        k, n = wT.shape
        return np.ascontiguousarray(wT.reshape(k // 128, 128, n).transpose(1, 0, 2))

    w_in = arr(L0_attn_w_in).reshape(H, 3, 16, D)
    b_in = arr(L0_attn_b_in).reshape(H, 3, 16)
    w5 = w_in.reshape(2, 8, 3, 16, D).transpose(2, 0, 3, 1, 4)
    b5 = b_in.reshape(2, 8, 3, 16).transpose(2, 0, 3, 1)
    wqk = chunks(w5[0:2].reshape(512, D).T)
    bqk = np.ascontiguousarray(b5[0:2].reshape(4, 128).T)
    wv = chunks(w_in[:, 2].reshape(256, D).T)
    bv = b_in[:, 2].reshape(256)
    wout = chunks(arr(L0_attn_w_out).T)
    lora_a = arr(L0_ffn_lora_A).reshape(E * R, D)
    wgate = chunks(np.concatenate([arr(L0_ffn_gate_W), lora_a]).T)
    wi = chunks(arr(L0_ffn_wi_W).T)
    wo = chunks(arr(L0_ffn_wo_W).T)
    lora_b = np.transpose(arr(L0_ffn_lora_B), (0, 2, 1)).reshape(E * R, F)
    lora = np.concatenate([lora_b, lora_b, lora_b])
    wib = np.stack([arr(L0_ffn_wi_b)] * 2)
    brows = np.concatenate([bv, arr(L0_attn_b_out), arr(L0_ffn_wo_b), arr(L0_ffn_gate_b),
                            np.zeros(E * R, np.float32)])[None, :]
    ins = {"x": arr(L0_attn_x), "wqk": wqk, "wv": wv, "bqk": bqk, "wout": wout, "wgate": wgate, "wi": wi,
           "lora": lora, "wib": wib, "wo": wo, "brows": brows, "ident": np.eye(128, dtype=np.float32)}
    nc = bacc.Bacc("TRN2", target_bir_lowering=False, num_devices=1)
    arrays, aps = {}, []
    for name, a in ins.items():
        a = np.ascontiguousarray(a)
        arrays["in_" + name] = a
        aps.append(nc.dram_tensor("in_" + name, a.shape, mybir.dt.from_np(a.dtype), kind="ExternalInput").ap())
    aps.append(nc.dram_tensor("out_y", (B, L, D), F32, kind="ExternalOutput").ap())
    sandwich(nc, *aps)
    r = run_bass_kernel_spmd(nc, [arrays], core_ids=[0])
    return r.results[0]["out_y"]
```

```python
from contextlib import ExitStack

import numpy as np
import concourse.bass as bass
from concourse import mybir

F32 = mybir.dt.float32
F32R = mybir.dt.float32r
BF16 = mybir.dt.bfloat16
ALU = mybir.AluOpType
ACT = mybir.ActivationFunctionType
AX_X = mybir.AxisListType.X

B, L, D, H, F, E, R = 8, 512, 256, 16, 1024, 8, 4
NT = L // 128
EPS = 1e-5
PIECES = 5
XB = 4
HEADS = 64
NS = 6
DMA_LATENCY = 2.5
START, WINDOW, LEAD, EVAC = 76.15, 43.53, 4.311, 11.49
PRE_PACE, PRE1_AT, PRE_AT, POST_PACE = 2.35, -18.7, 17.99, 1.39
FEED_PACE = 1.75
LATE_PACE, LATE_AT, POOL_AT, LOAD_LATENCY = 5.63, -96.17, 7.14, 12
PE_SLACK, AC_SLACK, DV_SLACK, PO_SLACK = 0, 0.13, 0.17, 1.34
PERIOD, WARM = 3.41, 1.27


class Point:

    def __init__(self, sem, n, t, engine=None):
        self.sem, self.n, self.t, self.engine = sem, n, t, engine


class Queue:

    def __init__(self, out=0.1, slack=0.0, into=0.0):
        self.items, self.seen, self.t = [], {}, 0.0
        self.out, self.slack, self.into = out, slack, into

    def do(self, fn, sem=None, by=1, late=0.0):
        if sem is None:
            self.items.append(fn)
            return None
        sem[1] += by
        self.items.append(lambda e: fn(e).then_inc(sem[0], by))
        return Point(sem, sem[1], self.t + late, self)

    def wait(self, *points):
        for p in points:
            if self.seen.get(id(p.sem), 0) < p.n:
                self.seen[id(p.sem)] = p.n
                self.items.append(lambda e, s=p.sem[0], v=p.n: e.wait_ge(s, v))

    def spend(self, begin, cost, share=1.0):
        return cost

    def play(self, e):
        for fn in self.items:
            fn(e)


class Array(Queue):

    def __init__(self, *a):
        super().__init__(*a)
        self.work = {}

    def spend(self, begin, cost, share=1.0):
        n = int(begin / PERIOD)
        busy = cost * share
        if self.work.get(n - 1, 0.0) < WARM:
            cost *= 2
        beyond = max(0.0, begin + cost - (n + 1) * PERIOD) / cost * busy
        self.work[n] = self.work.get(n, 0.0) + busy - beyond
        self.work[n + 1] = self.work.get(n + 1, 0.0) + beyond
        return cost


class Order:

    def __init__(self):
        self.streams, self.target = [], 0.0

    def start(self, gen, pace, target):
        want = next(gen, None)
        if want is not None:
            self.streams.append([target, pace, gen, want])

    def alone(self, gen):
        for engine, cost, points in gen:
            pts = points()
            engine.wait(*pts)
            engine.t = max([engine.t] + [p.t + p.engine.out for p in pts]) + cost

    def run(self):
        while self.streams:
            first, ready = {}, []
            for s in self.streams:
                engine, cost, points = s[3][:3]
                pts = points()
                if pts is None:
                    continue
                begin = max([engine.t] + [p.t + max(p.engine.out if p.engine else 0.2, engine.into) for p in pts])
                ready.append((begin, s, pts))
                first[engine] = min(first.get(engine, begin), begin)
            pick = {}
            for begin, s, pts in ready:
                engine = s[3][0]
                if begin <= first[engine] + engine.slack and (engine not in pick or s[0] < pick[engine][1][0]):
                    pick[engine] = (begin, s, pts)
            begin, s, pts = min(pick.values(), key=lambda v: v[0])
            engine, cost, _, *share = s[3]
            engine.t = begin + engine.spend(begin, cost, *share)
            engine.wait(*pts)
            self.target = s[0]
            want = next(s[2], None)
            if want is None:
                self.streams.remove(s)
            else:
                s[0] += s[1] * cost
                s[3] = want


def have(*cells):
    def points():
        out = []
        for c, n in cells:
            if len(c) < n:
                return None
            out += c
        return out
    return points


def sandwich(nc, x, wqk, wv, bqk, wout, wgate, wi, lora, wib, wo, brows, bg, ident, out):
    with ExitStack() as ctx:
        def sb(name, shape, dt=F32):
            return ctx.enter_context(nc.sbuf_tensor(name, shape, dt))

        def sem(name):
            return [ctx.enter_context(nc.semaphore(name)), 0]

        ps = [ctx.enter_context(nc.psum_tensor(f"ps{i}", [128, 512], F32)) for i in range(NS)]
        pu = [ctx.enter_context(nc.psum_tensor(f"pu{i}", [128, 512], F32)) for i in range(8 - NS)]

        xb = sb("xb", [128, XB, NT, D])
        xn = sb("xn", [128, NT, D])
        xnT = sb("xnT", [128, 2, 2, L], F32R)
        qk = sb("qk", [128, 4, 2, L], F32R)
        stack = sb("stack", [128, PIECES, 2, 2, L], F32R)
        vo = sb("vo", [128, 2, NT, D])
        oT = sb("oT", [128, 2, L])
        y = sb("y", [128, NT, D])
        y2 = sb("y2", [128, NT, D])
        yT = sb("yT", [128, 2, 2, L], F32R)
        inter = sb("inter", [128, 2, 8, L], F32R)
        wqk_r = sb("wqk_r", [128, 2, 2, 512], F32R)
        wv_r = sb("wv_r", [128, 2, 2, 256], F32R)
        wg_r = sb("wg_r", [128, 2, 2, 40], F32R)
        wi_r = sb("wi_r", [128, 2, 2, F], F32R)
        wo_r = sb("wo_r", [128, 2, 8, D], F32R)
        lb_r = sb("lb_r", [98, F], F32R)
        br_r = sb("br_r", [3, 768], BF16)
        wout_s = sb("wout_s", [128, 2, D])
        bqk_s = sb("bqk_s", [128, 4])
        wg_s = sb("wg_s", [128, 2, 40])
        bg_s = sb("bg_s", [40, 1])
        id_s = sb("id_s", [128, 128])
        ones_r = sb("ones_r", [3, 128], BF16)
        halves = sb("halves", [128, NT])
        w8 = sb("w8", [128, NT, E])
        nmax = sb("nmax", [128, 8])
        ssum = sb("ssum", [128, 2, NT, H])
        srec = sb("srec", [128, NT, H])
        sone = sb("sone", [128, NT, H])
        st6 = [sb(f"st6_{i}", [128, NT, 6]) for i in range(3)]
        mv = [sb(f"mv_{i}", [128, NT, 2]) for i in range(3)]
        nmr = [sb(f"nmr_{i}", [128, 3, NT]) for i in range(3)]
        gs = sb("gs", [128, NT, 40])
        g8 = sb("g8", [128, 6, NT, E])
        g1 = sb("g1", [128, 5, NT])
        ml = sb("ml", [128, NT, E, R])
        mh = sb("mh", [128, NT, 32], F32R)
        ms = sb("ms", [128, NT, 98])
        lt_r = sb("lt_r", [98, L], F32R)

        s_w = [sem(f"s_w{i}") for i in range(12)]
        s_x = [sem(f"s_x{i}") for i in range(XB)]
        s_st = [sem(f"s_st{i}") for i in range(PIECES)]
        s_out = [sem(f"s_out{i}") for i in range(XB + 1)]
        s_row = sem("s_row")
        s_const = sem("s_const")
        s_split_v = sem("s_split_v")
        s_split_a = sem("s_split_a")
        s_split_p = sem("s_split_p")
        s_score = sem("s_score")
        s_max = sem("s_max")
        s_exp = sem("s_exp")
        s_unit = sem("s_unit")
        s_high_a = sem("s_high_a")
        s_low_v = sem("s_low_v")
        s_high = sem("s_high")
        s_low = sem("s_low")
        s_whole = sem("s_whole")
        s_stat = sem("s_stat")
        s_norm_v = sem("s_norm_v")
        s_norm = sem("s_norm")
        s_ratio = sem("s_ratio")
        s_gate = sem("s_gate")
        s_gexp = sem("s_gexp")

        PE, AC, DV, PO, SP = Array(0.2, PE_SLACK), Queue(0.1, AC_SLACK), Queue(0.13, DV_SLACK), Queue(0.1, PO_SLACK), Queue(0.1)
        order = Order()

        def load(i, dst, src):
            return SP.do(lambda e: e.dma_start(dst, src), s_w[i], 16, late=4.0 if i < 5 else LOAD_LATENCY)

        x_here, x_free = {}, {i: [] for i in range(B)}

        def load_x(b):
            x_here[b] = SP.do(lambda e: e.dma_start(
                xb[:, b % XB], x[b].rearrange("(t p) d -> p t d", p=128)), s_x[b % XB], 16, late=4.0)

        load_x(0)
        wqk_st = oT[:].rearrange("p a b -> p (a b)").rearrange("p (c m) -> p c m", c=2)
        wv_st = y[:, 0:2, :]
        c_wqk = load(0, wqk_st, wqk)
        c_id = load(1, id_s[:], ident)
        c_bqk = load(2, bqk_s[:], bqk)
        c_wv = load(3, wv_st, wv)
        rows_st = y2[0:1, 0:3, :].rearrange("p a b -> p (a b)")
        c_rows = load(4, rows_st, brows)
        load_x(1)
        wi_st = vo[:, 1, :, :].rearrange("p a b -> p (a b)")
        wo_st = xb[:, 2:4].rearrange("p x t d -> p (x t d)").rearrange("p (f d) -> p f d", f=8)
        c_wo = load(5, wo_st, wo)
        c_wi0 = load(6, wi_st, wi[:, 0, :])
        c_wg = load(8, wg_s[:], wgate)
        c_bg = load(11, bg_s[:], bg)
        c_wout = load(9, wout_s[:], wout)

        PO.do(lambda e: e.memset(ones_r[:], 1.0), s_const)
        PO.do(lambda e: e.memset(halves[:], -0.5), s_const)
        for i in range(E):
            PO.do(lambda e, i=i: e.memset(w8[:, :, i:i + 1], float(E - i)), s_const)
        c_const = PO.do(lambda e: e.memset(ms[:, :, 96:98], 1.0), s_const)

        norm_free = [[], [], []]
        nmr_here = {}
        ALL, HALVES = (0, 1, 2, 3), ((0, 1), (2, 3))

        def mean_rstd(i, src, points, ts=ALL):
            n = slice(ts[0], ts[-1] + 1)
            for t in ts:
                yield DV, 0.335, lambda: None if points() is None else points() + norm_free[i]
                a = DV.do(lambda e, t=t: e.bn_stats(st6[i][:, t, :], src[:, t, :]), s_stat)
            yield DV, 0.3, lambda: [a]
            for t in ts:
                a = DV.do(lambda e, t=t: e.bn_aggr(mv[i][:, t, :], st6[i][:, t, :]), s_stat)
            yield PO, 0.4, lambda: [a, c_const]
            PO.do(lambda e: e.tensor_scalar(nmr[i][:, 0, n], mv[i][:, n, 0], -1.0, None, ALU.mult), s_norm)
            a = PO.do(lambda e: e.tensor_scalar(nmr[i][:, 1, n], mv[i][:, n, 1], EPS, None, ALU.add), s_norm)
            yield PO, 0.96, lambda: [a]
            a = PO.do(lambda e: e.tensor_tensor(nmr[i][:, 2, n], nmr[i][:, 1, n], halves[:, n], ALU.pow), s_norm)
            nmr_here[i, ts] = a
            if ts == ALL:
                norm_free[i] = [a]

        def norm(i, dst, src, points, got, ts=ALL, q=None):
            q = q or PO
            for t in ts:
                yield q, 0.54 if q is PO else 0.323, lambda: None if points() is None else points() + [nmr_here[i, ts]]
                p = q.do(lambda e, t=t: e.tensor_scalar(dst[:, t, :], src[:, t, :], nmr[i][:, 0, t:t + 1],
                                                        nmr[i][:, 2, t:t + 1], ALU.add, ALU.mult),
                         s_norm if q is PO else s_norm_v)
            if ts == ALL:
                norm_free[i] = [p]
            got.append(p)

        xn_here = []
        PO.t = DV.t = 4.0
        order.alone(mean_rstd(0, xb[:, 0], lambda: [x_here[0]]))
        order.alone(norm(0, xn, xb[:, 0], lambda: [], xn_here))

        PO.wait(c_rows)
        rest = y2[0:1, 3, :]
        rows23 = vo[0:1, 0].rearrange("p a b -> p (a b)").bitcast(BF16).rearrange("p (a b) -> p a b", a=2)
        for i in range(3):
            n = slice(256 * i, 256 * i + 256)
            a = PO.do(lambda e, n=n: e.tensor_copy(br_r[0:1, n], rows_st[:, n]), s_split_p)
            PO.wait(a)
            a = PO.do(lambda e, n=n: e.tensor_tensor(rest, rows_st[:, n], br_r[0:1, n], ALU.subtract), s_split_p)
            PO.wait(a)
            a = PO.do(lambda e, n=n: e.tensor_copy(rows23[:, 0, n], rest), s_split_p)
            PO.wait(a)
            c_rest = PO.do(lambda e, n=n: e.tensor_tensor(rows23[:, 1, n], rest, rows23[:, 0, n], ALU.subtract),
                           s_split_p)
            PO.wait(c_rest)

        DV.wait(c_wqk)
        for (lo, hi, k) in ((0, 256, 0.25), (256, 512, 1.0)):
            a = DV.do(lambda e, lo=lo, hi=hi, k=k: e.tensor_scalar(
                wqk_r[:, 0, :, lo:hi], wqk_st[:, :, lo:hi], k, None, ALU.mult), s_split_v)
            DV.wait(a)
            c_sqk = DV.do(lambda e, lo=lo, hi=hi, k=k: e.scalar_tensor_tensor(
                wqk_r[:, 1, :, lo:hi], wqk_st[:, :, lo:hi], k, wqk_r[:, 0, :, lo:hi].bitcast(F32),
                ALU.mult, ALU.subtract), s_split_v)
        DV.wait(c_bqk)
        c_bq = DV.do(lambda e: e.tensor_scalar(bqk_s[:, 0:2], bqk_s[:, 0:2], 0.25, None, ALU.mult), s_split_v)

        def split(q, sem_, high, low, whole):
            a = q.do(lambda e: e.tensor_copy(high, whole), sem_)
            q.wait(a)
            return q.do(lambda e: e.tensor_tensor(low, whole, high.bitcast(F32), ALU.subtract), sem_)

        DV.wait(c_wv)
        c_sv = split(DV, s_split_v, wv_r[:, 0], wv_r[:, 1], wv_st)
        SP.wait(c_rest)
        for i in range(2):
            c_brow = SP.do(lambda e, i=i: e.dma_start(br_r[i + 1:i + 2, :], rows23[:, i, 0:768]), s_row, 16)
        BV, BO, BW = (slice(0, 256), slice(256, 512), slice(512, 768))
        rl = inter[0:1, 0, 0:2, :].rearrange("p a b -> p (a b)")
        for q in (PE, AC, DV, SP):
            q.t = 8.0
        PO.t = POOL_AT
        c_const.t = c_rest.t = c_sv.t = c_sqk.t = c_bq.t = 8.0
        c_brow.t = POOL_AT + 2

        w_wo, w_wi, w_wg, w_lb = [], [], [], []
        v_free = {b: [] for b in range(B)}

        def base(b):
            return START + WINDOW * b

        def late_weights():
            def part(high, low, whole, pts, done):
                yield AC, 0.52, lambda: pts
                a = AC.do(lambda e: e.activation(high, whole, ACT.Copy), s_split_a)
                yield DV, 0.6, lambda: [a]
                done.append(DV.do(lambda e: e.tensor_tensor(low, whole, high.bitcast(F32), ALU.subtract), s_split_v))
            for i in range(2):
                got = []
                sl = slice(512 * i, 512 * i + 512)
                yield from part(wi_r[:, 0, 0, sl], wi_r[:, 1, 0, sl], wi_st[:, sl], [c_wi0], got)
            yield SP, 0.45, lambda: [got[-1]]
            c = load(7, wi_st, wi[:, 1, :])
            g2 = []
            yield from part(wg_r[:, 0], wg_r[:, 1], wg_s[:], [c_wg], g2)
            w_wg.append(g2[0])
            for i in range(4):
                got = []
                sl = slice(2 * i, 2 * i + 2)
                yield from part(wo_r[:, 0, sl], wo_r[:, 1, sl], wo_st[:, sl], [c_wo], got)
            w_wo.append(got[0])
            x_free[2].append(got[0])
            x_free[3].append(got[0])
            for i in range(2):
                got = []
                sl = slice(512 * i, 512 * i + 512)
                yield from part(wi_r[:, 0, 1, sl], wi_r[:, 1, 1, sl], wi_st[:, sl], [c], got)
            w_wi.append(got[0])
            v_free[1].append(got[0])
            lst = y2[0:98].rearrange("p a b -> p (a b)")
            yield SP, 0.9, lambda: [c_sv, c_rest]
            load(10, lst[0:96], lora)
            c2 = load(10, lst[96:98], wib)
            for i in range(2):
                sl = slice(512 * i, 512 * i + 512)
                yield AC, 0.52, lambda: [c2]
                a = AC.do(lambda e, sl=sl: e.activation(lb_r[:, sl], lst[:, sl], ACT.Copy), s_split_a)
            yield DV, 1.1, lambda: [a]
            a = DV.do(lambda e: e.tensor_tensor(rl[:, :], lst[96:97], lb_r[96:97].bitcast(F32), ALU.subtract),
                      s_split_v)
            yield DV, 1.1, lambda: [a]
            z = DV.do(lambda e: e.tensor_tensor(lb_r[32:64], lst[32:64], lb_r[32:64].bitcast(F32), ALU.subtract),
                      s_split_v)
            yield SP, 0.45, lambda: [z, c_brow]
            w_lb.append(SP.do(lambda e: e.dma_start(lb_r[97:98].bitcast(F32), rl[:, :].bitcast(F32)), s_row, 16,
                              late=DMA_LATENCY))
            y2_free[-1].append(z)

        bank_free = [[] for _ in pu]
        bank_taken = [False for _ in pu]

        def unit(pieces, evac, points=lambda: [], keep=0):
            def pick():
                return min((i for i in range(len(pu)) if not bank_taken[i]),
                           key=lambda i: max([p.t for p in bank_free[i]], default=0.0))

            def cond():
                pts = points()
                return None if pts is None or bank_taken.count(False) <= keep else pts + bank_free[pick()]
            for n, (cost, piece, *more) in enumerate(pieces):
                yield PE, cost, cond if n == 0 else more[0] if more else lambda: []
                if n == 0:
                    i = pick()
                    bank_taken[i] = True
                done = piece(pu[i])

            def release(*pts):
                bank_free[i] = list(pts)
                bank_taken[i] = False
            order.start(evac(pu[i], done, release), 1.0, order.target - EVAC)

        def mm(out_, lhsT, rhs, start, stop, sem_=None):
            return PE.do(lambda e: e.matmul(out_, lhsT, rhs, start=start, stop=stop), sem_)

        def three(out_, lT, r, chunks, first=True, last=False, sem_=None):
            n = len(chunks)
            for i, c in enumerate(chunks):
                for j, (a, b_) in enumerate(((0, 0), (0, 1), (1, 0))):
                    end = last and i == n - 1 and j == 2
                    p = mm(out_, lT(a, c), r(b_, c), first and i == 0 and j == 0, end, sem_ if end else None)
            return p

        def transposes(src, c):
            def pe(bank):
                for t in range(NT):
                    p = PE.do(lambda e, t=t: e.transpose(bank[:, t * 128:(t + 1) * 128],
                                                         src[:, t, c * 128:(c + 1) * 128], id_s[:]),
                              s_unit if t == NT - 1 else None)
                return p
            return pe

        def high_low(high, low, free, got, relu=False):
            def evac(bank, done, release):
                yield AC, 0.478, lambda: [done] + free
                h = AC.do(lambda e: e.activation(high, bank[:], ACT.Relu if relu else ACT.Copy), s_high)
                yield DV, 0.602, lambda: [h]
                if relu:
                    p = DV.do(lambda e: e.scalar_tensor_tensor(low, bank[:], 0.0, high.bitcast(F32), ALU.max,
                                                               ALU.subtract), s_low)
                else:
                    p = DV.do(lambda e: e.tensor_tensor(low, bank[:], high.bitcast(F32), ALU.subtract), s_low)
                release(p)
                got.append(p)
            return evac

        def high_low_biased(high, low, bias, free, got):
            def evac(bank, done, release):
                yield AC, 0.571, lambda: [done, c_bq] + free
                h = AC.do(lambda e: e.activation(high, bank[:], ACT.Identity, bias=bias), s_high)
                yield DV, 0.663, lambda: [h, c_bq]
                p = DV.do(lambda e: e.scalar_tensor_tensor(low, bank[:], bias, high.bitcast(F32), ALU.add,
                                                           ALU.subtract), s_low)
                release(p)
                got.append(p)
            return evac

        def copied(dst, got, points=lambda: []):
            def evac(bank, done, release):
                yield AC, 0.478, lambda: None if points() is None else [done] + points()
                p = AC.do(lambda e: e.activation(dst, bank[:], ACT.Copy), s_whole)
                release(p)
                got.append(p)
            return evac

        def add_norm(i, w, xs, points, got, ts=ALL, q=None):
            q = q or PO
            yield from mean_rstd(i, w, points, ts)
            n = []
            yield from norm(i, w, w, lambda: [], n, ts, q)
            for t in ts:
                yield q, 0.687 if q is PO else 0.31, lambda: n
                p = q.do(lambda e, t=t: e.tensor_tensor(xs[:, t, :], xs[:, t, :], w[:, t, :], ALU.add),
                         s_norm if q is PO else s_norm_v)
            got.append(p)

        def cells(n=B):
            return {i: [] for i in range(-2, n)}

        xn_read, xnT_read, qk_read, v_here, v_read = cells(), cells(), cells(), cells(), cells()
        y_free, yT_read, lt_read, inter_read, y2_free = (cells() for _ in range(5))
        gates_free, ms_read, gT_read, exp_done, ssum_free = (cells() for _ in range(5))
        fed = cells()
        y_free[0].append(c_sv)
        piece_here = {p: [] for p in range(4 * B)}
        piece_read = {p: [] for p in range(-PIECES, 4 * B)}
        v_read[-2].append(c_brow)

        def prior(c, b, n=1):
            return lambda: None if b >= 0 and len(c[b]) < n else c[b]

        def both(*fs):
            def points():
                out = []
                for f in fs:
                    v = f()
                    if v is None:
                        return None
                    out += v
                return out
            return points

        def stacks(b, parts):
            for j in range(4):
                piece = 4 * b + j
                ring = piece % PIECES
                for p in range(2):
                    for t in range(4):
                        yield SP, 0.65, both(lambda: parts, prior(piece_read, piece - PIECES))
                        qa, ka, s = t // 2, 2 + t % 2, 2 * j + p
                        dst = stack[64 * p + t:64 * p + 64:4, ring].rearrange("p q c l -> p q (c l)")
                        src = qk[s:128:8, qa:ka + 1:ka - qa].rearrange("p q c l -> p q (c l)")
                        z = SP.do(lambda e, dst=dst, src=src: e.dma_start(dst.bitcast(F32), src.bitcast(F32)),
                                  s_st[ring], 16, late=DMA_LATENCY)
                piece_here[piece].append(z)
                qk_read[b].append(z)

        def loads():
            for b in range(2, B):
                yield SP, 0.45, (prior(x_free, b) if b in (2, 3) else prior(fed, b - XB))
                load_x(b)

        def pre(b):
            xs = xb[:, b % XB]
            n = xn_here
            if b:
                yield from mean_rstd(0, xs, lambda: [x_here[b]] if b in x_here else None)
                n = []
                yield from norm(0, xn, xs, prior(xn_read, b - 1), n)
            hl, parts = [], []
            for c in range(2):
                yield from unit([(0.45, transposes(xn, c))],
                                high_low(xnT[:, 0, c], xnT[:, 1, c], xnT_read[b - 1], hl),
                                both(lambda: n + [c_id], prior(xnT_read, b - 1)))
            xn_read[b].append(Point(s_unit, s_unit[1], PE.t))
            for m in range(4):
                part, c = m // 2, m % 2

                def pe(bank, m=m):
                    PE.wait(c_sqk)
                    return three(bank[:], lambda a, k: wqk_r[:, a, k, m * 128:(m + 1) * 128],
                                 lambda a, k: xnT[:, a, k, :], (0, 1), last=True, sem_=s_unit)
                yield from unit([(1.29, pe)], high_low_biased(qk[:, 2 * part, c], qk[:, 2 * part + 1, c],
                                                              bqk_s[:, m:m + 1], qk_read[b - 1], parts),
                                both(have((hl, 2)), prior(qk_read, b - 1, 4)))
            vs = []
            for u in range(2):
                def pe(bank, k, u=u):
                    PE.wait(c_sv, c_brow, c_const)
                    t = 2 * u + k
                    o = bank[:, k * 256:(k + 1) * 256]
                    three(o, lambda a, c: xnT[:, a, c, t * 128:(t + 1) * 128], lambda a, c: wv_r[:, a, c, :], (0, 1))
                    return mm(o, ones_r[:], br_r[:, BV], False, True, s_unit)
                yield from unit([(0.77, lambda bk, pe=pe: pe(bk, 0)), (0.77, lambda bk, pe=pe: pe(bk, 1))],
                                copied(vo[:, b % 2, 2 * u:2 * u + 2, :].rearrange("p a b -> p (a b)"), v_here[b],
                                       prior(v_read, b - 2) if b != 1 else prior(v_free, 1)),
                                prior(v_read, b - 2) if b != 1 else prior(v_free, 1))
            xnT_read[b].append(Point(s_unit, s_unit[1], PE.t))
            yield SP, 0.0, have((parts, 4))
            order.start(stacks(b, parts), 0.0, order.target - 5)
            yield SP, 0.0, lambda: []
            if b + 1 < B:
                order.start(pre(b + 1), PRE_PACE, base(b) + (PRE_AT if b else PRE1_AT))

        def post(b):
            xs = xb[:, b % XB]
            v = vo[:, b % 2]
            yield DV, 0.47, both(prior(exp_done, b), prior(v_read, b - 1))
            a = DV.do(lambda e: e.reciprocal(srec[:], ssum[:, b % 2]), s_ratio)
            yield DV, 0.13, lambda: [a]
            a = DV.do(lambda e: e.tensor_tensor(sone[:], ssum[:, b % 2], srec[:], ALU.mult), s_ratio)
            ssum_free[b].append(a)
            o, end = {}, b == B - 1
            for t in range(NT):
                q = DV if end and t % 2 else PO
                yield q, 0.6 if q is PO else 0.31, both(lambda: [a], prior(v_here, b, 2))
                vt = v[:, t, :].rearrange("p (h d) -> p h d", h=H)
                o[q] = q.do(lambda e, vt=vt, t=t: e.tensor_tensor(
                    vt, vt, sone[:, t, :].unsqueeze(2).to_broadcast([128, H, 16]), ALU.mult),
                    s_norm if q is PO else s_norm_v)
            got = []
            for c in range(2):
                yield from unit([(0.45, transposes(v, c))],
                                copied(oT[:, c, :], got, prior(gT_read, b - 1)),
                                both(lambda: list(o.values()), prior(gT_read, b - 1)))
            v_read[b].append(Point(s_unit, s_unit[1], PE.t))
            ys = []
            for u in range(2):
                def pe(bank, k, u=u):
                    PE.wait(c_wout, c_brow, c_const)
                    t = 2 * u + k
                    o_ = bank[:, k * 256:(k + 1) * 256]
                    for c in range(2):
                        mm(o_, oT[:, c, t * 128:(t + 1) * 128], wout_s[:, c, :], c == 0, False)
                    return mm(o_, ones_r[:], br_r[:, BO], False, True, s_unit)
                yield from unit([(1.0, lambda bk, pe=pe: pe(bk, 0)), (1.0, lambda bk, pe=pe: pe(bk, 1))],
                                copied(y[:, 2 * u:2 * u + 2, :].rearrange("p a b -> p (a b)"), ys,
                                       prior(y_free, b)), both(have((got, 2)), prior(y_free, b)))
            oT_read = [Point(s_unit, s_unit[1], PE.t)]
            n = []

            def norms(ts, points, q):
                x1 = []
                yield from add_norm(1, y, xs, points, x1, ts, q)
                yield from mean_rstd(1, xs, lambda: x1, ts)
                yield from norm(1, y, xs, lambda: [], n, ts, q)
            if end:
                for u, ts in enumerate(HALVES):
                    order.start(norms(ts, lambda u=u: None if len(ys) <= u else [ys[u]], DV), POST_PACE, order.target)
            else:
                yield from norms(ALL, have((ys, 2)), PO)
            hl = []
            for c in range(2):
                yield from unit([(0.45, transposes(y, c))],
                                high_low(yT[:, 0, c], yT[:, 1, c], yT_read[b - 1], hl),
                                both(have((n, 2 if end else 1)), prior(yT_read, b - 1)))
            if b + 1 < B:
                y_free[b + 1].append(Point(s_unit, s_unit[1], PE.t))
            gd, lt = [], []
            if end:
                order.start(feed(b, lt, hl), FEED_PACE, order.target + 1)
            gT = oT[0:40, 0, :]

            def evac(bank, done, release):
                yield AC, 0.571, lambda: [done, c_bg] + oT_read
                p = AC.do(lambda e: e.activation(gT, bank[0:40, :], ACT.Identity, bias=bg_s[:, 0:1]), s_whole)
                release(p)
                gd.append(p)
            yield from unit([(1.29, lambda bank: three(
                bank[0:40, :], lambda a_, c: wg_r[:, a_, c, :], lambda a_, c: yT[:, a_, c, :], (0, 1), last=True,
                sem_=s_unit))], evac, both(have((hl, 2)), have((w_wg, 1))))

            def pe(bank):
                for t in range(NT):
                    p = PE.do(lambda e, t=t: e.transpose(bank[:, t * 40:(t + 1) * 40], gT[:, t * 128:(t + 1) * 128],
                                                         id_s[0:40, 0:40]), s_unit if t == NT - 1 else None)
                gT_read[b].append(p)
                return p

            def evac(bank, done, release):
                yield DV, 0.23, both(lambda: [done], prior(gates_free, b - 1))
                p = DV.do(lambda e: e.tensor_copy(gs[:].rearrange("p t g -> p (t g)"), bank[:, 0:160]), s_gate)
                release(p)
                gd.append(p)
            yield from unit([(0.2, pe)], evac, have((gd, 1)))

            def wide(i):
                return g1[:, i, :].unsqueeze(2).to_broadcast([128, NT, E])
            lg = gs[:, :, 0:8]
            last = [None]

            def dv(fn, cost=0.1):
                pts = have((gd, 2)) if last[0] is None else lambda: [last[0]]
                yield DV, cost, pts
                last[0] = DV.do(fn, s_gate)
            yield from dv(lambda e: e.tensor_reduce(g1[:, 0, :], lg, AX_X, ALU.max))
            yield from dv(lambda e: e.tensor_tensor(g8[:, 0], lg, wide(0), ALU.subtract))
            yield AC, 0.12, lambda: [last[0]]
            last[0] = AC.do(lambda e: e.activation(g8[:, 1], g8[:, 0], ACT.Exp), s_gexp)
            yield from dv(lambda e: e.tensor_reduce(g1[:, 1, :], g8[:, 1], AX_X, ALU.add))
            yield from dv(lambda e: e.reciprocal(g1[:, 2, :], g1[:, 1, :]))
            yield from dv(lambda e: e.tensor_tensor(g8[:, 2], g8[:, 1], wide(2), ALU.mult))
            yield from dv(lambda e: e.tensor_reduce(g1[:, 3, :], g8[:, 2], AX_X, ALU.max))
            yield from dv(lambda e: e.tensor_tensor(g8[:, 3], g8[:, 2], wide(3), ALU.is_equal))
            yield from dv(lambda e: e.tensor_tensor(g8[:, 4], g8[:, 3], w8[:], ALU.mult))
            yield from dv(lambda e: e.tensor_reduce(g1[:, 4, :], g8[:, 4], AX_X, ALU.max))
            yield from dv(lambda e: e.tensor_tensor(g8[:, 5], g8[:, 4], wide(4), ALU.is_equal))
            yield from dv(lambda e: e.tensor_tensor(ml[:], gs[:, :, 8:40].rearrange("p t (e r) -> p t e r", e=E),
                                                    g8[:, 5].unsqueeze(3).to_broadcast([128, NT, E, R]), ALU.mult),
                          0.2)
            mlf = ml[:].rearrange("p t e r -> p t (e r)")
            yield from dv(lambda e: e.tensor_copy(mh[:], mlf), 0.2)
            yield DV, 0.5, both(lambda: [last[0]], prior(ms_read, b - 1))
            for k in range(2):
                DV.do(lambda e, k=k: e.tensor_copy(ms[:, :, 32 * k:32 * k + 32], mh[:].bitcast(F32)), s_gate)
            a = DV.do(lambda e: e.tensor_tensor(ms[:, :, 64:96], mlf, mh[:].bitcast(F32), ALU.subtract), s_gate)
            gates_free[b].append(a)

            def pe(bank):
                for t in range(NT):
                    p = PE.do(lambda e, t=t: e.transpose(bank[0:98, t * 128:(t + 1) * 128], ms[:, t, :], id_s[:]),
                              s_unit if t == NT - 1 else None)
                ms_read[b].append(p)
                return p

            def evac(bank, done, release):
                yield AC, 0.478, both(lambda: [done], prior(lt_read, b - 1))
                p = AC.do(lambda e: e.activation(lt_r[:], bank[0:98, :], ACT.Copy), s_whole)
                release(p)
                lt.append(p)
            yield from unit([(0.43, pe)], evac, lambda: [a])
            if not end:
                order.start(feed(b, lt, hl), FEED_PACE, order.target)
            yield SP, 0.0, lambda: []
            if b + 1 < B:
                order.start(post(b + 1), POST_PACE, base(b + 2))

        def feed(b, lt, hl):
            xs = xb[:, b % XB]
            got, end = [], b == B - 1
            for f in range(8):
                def without_lora(bank, f=f):
                    three(bank[:], lambda a_, c: wi_r[:, a_, c, f * 128:(f + 1) * 128],
                          lambda a_, c: yT[:, a_, c, :], (0, 1))

                def with_lora(bank, f=f):
                    return mm(bank[:], lb_r[:, f * 128:(f + 1) * 128], lt_r[:], False, True, s_unit)
                evac = high_low(inter[:, 0, f, :], inter[:, 1, f, :], inter_read[b - 1], got, True)
                here = both(have((hl, 2), (w_wi, 1), (w_lb, 1)), prior(inter_read, b - 1))
                if end:
                    order.start(unit([(1.29, without_lora), (0.22, with_lora, have((lt, 1)))], evac, here, 2), 0.0,
                                order.target + f)
                else:
                    yield from unit([(1.29, without_lora), (0.22, with_lora)], evac, both(have((lt, 1)), here))
            if end:
                yield SP, 0.0, have((got, 8))
            yT_read[b].append(Point(s_unit, s_unit[1], PE.t))
            lt_read[b].append(Point(s_unit, s_unit[1], PE.t))
            ys = []
            for u in range(2):
                def pe(bank, k, part, u=u):
                    t = 2 * u + k
                    o_ = bank[:, k * 256:(k + 1) * 256]
                    p = three(o_, lambda a_, f: inter[:, a_, f, t * 128:(t + 1) * 128],
                              lambda a_, f: wo_r[:, a_, f, :], range(4 * part, 4 * part + 4), first=part == 0)
                    return mm(o_, ones_r[:], br_r[:, BW], False, True, s_unit) if part else p
                yield from unit([(1.31 + 0.11 * h, lambda bk, pe=pe, k=k, h=h: pe(bk, k, h))
                                     for k in range(2) for h in range(2)],
                                copied(y2[:, 2 * u:2 * u + 2, :].rearrange("p a b -> p (a b)"), ys,
                                       prior(y2_free, b - 1)), both(have((got, 8), (w_wo, 1))))
            inter_read[b].append(Point(s_unit, s_unit[1], PE.t))

            def finish(ts, points, q):
                out_, n = [], slice(ts[0], ts[-1] + 1)
                yield from add_norm(2, y2, xs, points, out_, ts, q)
                y2_free[b].append(out_[0])
                yield SP, 0.45, lambda: out_
                fed[b].append(SP.do(lambda e: e.dma_start(
                    out[b].rearrange("(t p) d -> p t d", p=128)[:, n], xs[:, n]), s_out[XB if ts == HALVES[1] else b % XB], 16,
                    late=DMA_LATENCY))
            if end:
                for u, ts in enumerate(HALVES):
                    order.start(finish(ts, lambda u=u: None if len(ys) <= u else [ys[u]], DV), 1.0, order.target)
            else:
                yield from finish(ALL, have((ys, 2)), PO)

        score_done, max_done, head_done = {}, {}, {}

        def where(i):
            b, k = divmod(i, HEADS)
            return b, k // 16, k % 16 // 4, k % 4 // 2, k % 2

        def there(d, key, early=False):
            return lambda: [] if early else ([d[key]] if key in d else None)

        def scores():
            for i in range(B * HEADS):
                b, j, t, c, p = where(i)
                piece = 4 * b + j
                st = stack[64 * p:64 * p + 64, piece % PIECES]
                yield PE, 0.216, both(prior(piece_here, piece), there(head_done, i - NS, i < NS)), 0.5
                score_done[i] = PE.do(lambda e, st=st, i=i, c=c, t=t: e.matmul(
                    ps[i % NS][:], st[:, 0, c, t * 128:(t + 1) * 128], st[:, 1, c, :], start=True, stop=True),
                    s_score)
                if i % 16 == 15:
                    piece_read[piece].append(score_done[i])

        def maxima():
            for i in range(B * HEADS):
                yield DV, 0.598, both(there(score_done, i), there(head_done, i - 8, i < 8))
                max_done[i] = DV.do(lambda e, i=i: e.tensor_reduce(nmax[:, i % 8:i % 8 + 1], ps[i % NS][:], AX_X,
                                                                   ALU.max, negate=True), s_max)

        def exps():
            for i in range(B * HEADS):
                b, j, t, c, p = where(i)
                h = 8 * c + 2 * j + p
                yield AC, 0.664, both(there(max_done, i), prior(ssum_free, b - 2))
                head_done[i] = AC.do(lambda e, i=i, b=b, t=t, h=h: e.activation(
                    ps[i % NS][:], ps[i % NS][:], ACT.Exp, bias=nmax[:, i % 8:i % 8 + 1],
                    accum_out=ssum[:, b % 2, t, h:h + 1]), s_exp)
                if i % HEADS == HEADS - 1:
                    exp_done[b].append(head_done[i])
            for bank in ps:
                pu.append(bank)
                bank_free.append([head_done[i]])
                bank_taken.append(False)

        order.start(late_weights(), LATE_PACE, LATE_AT)
        order.start(pre(0), 0.0, -1000.0)
        order.start(loads(), 0.0, -1000.0)
        order.start(scores(), WINDOW / HEADS / 0.216, base(0) - LEAD)
        order.start(maxima(), WINDOW / HEADS / 0.598, base(0) - LEAD / 2)
        order.start(exps(), WINDOW / HEADS / 0.664, base(0))
        order.start(post(0), POST_PACE, base(1))
        order.run()
        SP.wait(*(p for b in range(B) for p in fed[b]))

        block = ctx.enter_context(nc.Block())

        @block.sync
        def _(e):
            SP.play(e)

        @block.tensor
        def _(e):
            PE.play(e)

        @block.scalar
        def _(e):
            AC.play(e)

        @block.vector
        def _(e):
            DV.play(e)

        @block.gpsimd
        def _(e):
            PO.play(e)


def kernel(L0_attn_x, L0_attn_w_in, L0_attn_b_in, L0_attn_w_out, L0_attn_b_out, L0_ffn_gate_W, L0_ffn_gate_b,
           L0_ffn_wi_W, L0_ffn_wi_b, L0_ffn_wo_W, L0_ffn_wo_b, L0_ffn_lora_A, L0_ffn_lora_B):
    import concourse.bacc as bacc
    from concourse.bass_utils import run_bass_kernel_spmd

    def arr(a):
        return np.asarray(a)

    def chunks(wT):
        k, n = wT.shape
        return np.ascontiguousarray(wT.reshape(k // 128, 128, n).transpose(1, 0, 2))

    w_in = arr(L0_attn_w_in).reshape(H, 3, 16, D)
    b_in = arr(L0_attn_b_in).reshape(H, 3, 16)
    w5 = w_in.reshape(2, 8, 3, 16, D).transpose(2, 0, 3, 1, 4)
    b5 = b_in.reshape(2, 8, 3, 16).transpose(2, 0, 3, 1)
    wqk = chunks(w5[0:2].reshape(512, D).T)
    bqk = np.ascontiguousarray(b5[0:2].reshape(4, 128).T)
    wv = chunks(w_in[:, 2].reshape(256, D).T)
    bv = b_in[:, 2].reshape(256)
    wout = chunks(arr(L0_attn_w_out).T)
    lora_a = arr(L0_ffn_lora_A).reshape(E * R, D)
    wgate = chunks(np.concatenate([arr(L0_ffn_gate_W), lora_a]).T)
    wi = chunks(arr(L0_ffn_wi_W).T)
    wo = chunks(arr(L0_ffn_wo_W).T)
    lora_b = np.transpose(arr(L0_ffn_lora_B), (0, 2, 1)).reshape(E * R, F)
    lora = np.concatenate([lora_b, lora_b, lora_b])
    wib = np.stack([arr(L0_ffn_wi_b)] * 2)
    brows = np.concatenate([bv, arr(L0_attn_b_out), arr(L0_ffn_wo_b)])[None, :]
    bg = np.concatenate([arr(L0_ffn_gate_b), np.zeros(E * R, np.float32)])[:, None]
    ins = {"x": arr(L0_attn_x), "wqk": wqk, "wv": wv, "bqk": bqk, "wout": wout, "wgate": wgate, "wi": wi,
           "lora": lora, "wib": wib, "wo": wo, "brows": brows, "bg": bg, "ident": np.eye(128, dtype=np.float32)}
    nc = bacc.Bacc("TRN2", target_bir_lowering=False, num_devices=1)
    arrays, aps = {}, []
    for name, a in ins.items():
        a = np.ascontiguousarray(a)
        arrays["in_" + name] = a
        aps.append(nc.dram_tensor("in_" + name, a.shape, mybir.dt.from_np(a.dtype), kind="ExternalInput").ap())
    aps.append(nc.dram_tensor("out_y", (B, L, D), F32, kind="ExternalOutput").ap())
    sandwich(nc, *aps)
    r = run_bass_kernel_spmd(nc, [arrays], core_ids=[0])
    return r.results[0]["out_y"]
```
